# Optimizing a Trainium2 kernel written in Bass

```python
import numpy as np
import jax
import jax.numpy as jnp

def _softmax(x, axis=-1):
    return jax.nn.softmax(x, axis=axis)

def _gelu(x):
    return jax.nn.gelu(x, approximate=True)

def _silu(x):
    return jax.nn.silu(x)

def _sigmoid(x):
    return jax.nn.sigmoid(x)

def _layernorm(x, axis=-1, eps=1e-05):
    m = jnp.mean(x, axis=axis, keepdims=True)
    v = jnp.var(x, axis=axis, keepdims=True)
    return (x - m) / jnp.sqrt(v + eps)

def _scatter_add(tgt, idx, src, axis=0):
    return tgt.at[idx].add(src)

def _segment_sum(src, seg, n):
    return jax.ops.segment_sum(src, seg, n)
kernel_name = 'mk_macaron_d1_jaxref_r4_470ffd'

def setup_inputs(seed: int=0):
    np.random.seed(seed)
    _w = jnp.asarray

    def _L0_attn_setup():
        import jax, jax.numpy as jnp
        import numpy as np
        B, T, C, H = (2, 512, 256, 16)
        D = C // H
        key = jax.random.key(seed)
        ks = jax.random.split(key, 5)
        s = 0.02
        return {'x': jax.random.normal(ks[0], (B, T, C), dtype=jnp.float32), 'W_attn': jax.random.normal(ks[1], (C, 3 * C), dtype=jnp.float32) * s, 'b_attn': jax.random.normal(ks[2], (3 * C,), dtype=jnp.float32) * s, 'W_proj': jax.random.normal(ks[3], (C, C), dtype=jnp.float32) * s, 'b_proj': jax.random.normal(ks[4], (C,), dtype=jnp.float32) * s}
    _L0_attn_in = _L0_attn_setup()

    def _L0_ffn_setup():
        import jax, jax.numpy as jnp
        import numpy as np
        N_EMBD = 256
        N_STATE = 1024
        key = jax.random.key(seed)
        k_x, k_w1, k_b1, k_w2, k_b2 = jax.random.split(key, 5)
        x = jax.random.normal(k_x, (4, 512, N_EMBD), dtype=jnp.float32)
        w1 = jax.random.normal(k_w1, (N_EMBD, N_STATE), dtype=jnp.float32) * (1.0 / np.sqrt(N_EMBD))
        b1 = jax.random.normal(k_b1, (N_STATE,), dtype=jnp.float32) * 0.02
        w2 = jax.random.normal(k_w2, (N_STATE, N_EMBD), dtype=jnp.float32) * (1.0 / np.sqrt(N_STATE))
        b2 = jax.random.normal(k_b2, (N_EMBD,), dtype=jnp.float32) * 0.02
        return {'x': x, 'w1': w1, 'b1': b1, 'w2': w2, 'b2': b2}
    _L0_ffn_in = _L0_ffn_setup()
    _d = {'L0_attn_x': _L0_attn_in['x'], 'L0_attn_W_attn': _L0_attn_in['W_attn'], 'L0_attn_b_attn': _L0_attn_in['b_attn'], 'L0_attn_W_proj': _L0_attn_in['W_proj'], 'L0_attn_b_proj': _L0_attn_in['b_proj'], 'L0_ffn_w1': _L0_ffn_in['w1'], 'L0_ffn_b1': _L0_ffn_in['b1'], 'L0_ffn_w2': _L0_ffn_in['w2'], 'L0_ffn_b2': _L0_ffn_in['b2']}
    _x0 = _d['L0_attn_x']
    _d['L0_attn_x'] = jax.random.normal(jax.random.fold_in(jax.random.key(seed), 1), (4, 2048, 256), dtype=_x0.dtype)
    del _x0
    return _d

def reference(L0_attn_x, L0_attn_W_attn, L0_attn_b_attn, L0_attn_W_proj, L0_attn_b_proj, L0_ffn_w1, L0_ffn_b1, L0_ffn_w2, L0_ffn_b2):

    def _L0_attn_ref(x, W_attn, b_attn, W_proj, b_proj):
        import jax, jax.numpy as jnp
        import numpy as np
        B, T, C, H = (2, 512, 256, 16)
        D = C // H
        Bb, Tt, Cc = x.shape
        kqv = x @ W_attn + b_attn
        q, k, v = jnp.split(kqv, 3, axis=2)
        q = q.reshape(Bb, Tt, H, D).transpose(0, 2, 1, 3)
        k = k.reshape(Bb, Tt, H, D).transpose(0, 2, 1, 3)
        v = v.reshape(Bb, Tt, H, D).transpose(0, 2, 1, 3)
        scale = 1.0 / jnp.sqrt(jnp.float32(D))
        att = jnp.einsum('bhqd,bhkd->bhqk', q, k) * scale
        causal = jnp.tril(jnp.ones((Tt, Tt), dtype=bool))
        att = jnp.where(causal[None, None], att, -jnp.inf)
        att = jax.nn.softmax(att, axis=-1)
        y = jnp.einsum('bhqk,bhkd->bhqd', att, v)
        y = y.transpose(0, 2, 1, 3).reshape(Bb, Tt, Cc)
        return y @ W_proj + b_proj

    def _L0_ffn_ref(x, w1, b1, w2, b2):
        import jax, jax.numpy as jnp
        import numpy as np
        N_EMBD = 256
        N_STATE = 1024
        h = jax.nn.gelu(jnp.einsum('bse,eh->bsh', x, w1) + b1, approximate=False)
        return jnp.einsum('bsh,he->bse', h, w2) + b2
    x = L0_attn_x
    x = x + 0.5 * _L0_ffn_ref(_layernorm(x, axis=-1), L0_ffn_w1, L0_ffn_b1, L0_ffn_w2, L0_ffn_b2)
    x = x + _L0_attn_ref(_layernorm(x, axis=-1), L0_attn_W_attn, L0_attn_b_attn, L0_attn_W_proj, L0_attn_b_proj)
    x = x + 0.5 * _L0_ffn_ref(_layernorm(x, axis=-1), L0_ffn_w1, L0_ffn_b1, L0_ffn_w2, L0_ffn_b2)
    return x

_drawn_inputs = setup_inputs


def setup_inputs(seed=0):
    import zlib

    import numpy as np

    out = dict(_drawn_inputs(seed))
    spreads = {}
    factors = {'L0_attn_W_attn': 4.101,
     'L0_attn_b_attn': 8.0,
     'L0_attn_W_proj': 3.988,
     'L0_attn_b_proj': 3.243,
     'L0_ffn_b1': 5.01,
     'L0_ffn_b2': 3.368}
    for name, (base, spread) in spreads.items():
        noise = np.random.default_rng([zlib.crc32(name.encode()), seed]).standard_normal(out[name].shape)
        drawn = base * np.exp(spread * noise) if base else spread * noise
        out[name] = jnp.asarray(drawn.astype(out[name].dtype))
    for name, factor in factors.items():
        out[name] = (out[name] * factor).astype(out[name].dtype)
    return out
```

```python
from contextlib import ExitStack

import concourse.bass as bass
from concourse import mybir

F32 = mybir.dt.float32
F32R = mybir.dt.float32r
ACT = mybir.ActivationFunctionType
ALU = mybir.AluOpType
AX = mybir.AxisListType

P = 128
B, T, C = 4, 2048, 256
H, D = 16, 16
F = 1024
EPS = 1e-5
KC = C // P
FT = F // P
NT = T // P
BLK = 512
NB = T // BLK
TPB = BLK // P
HG = 4
NG = H // HG
PAIRS = HG // 2
VW = D + 1
KS = 3 * D
KK = 2 * KS
KM = KK + 2
SCALE = float(D) ** -0.5
NEVER = -3.0e38

RING = 3
UPS = 4
ACCS = TPB
XNS = 4
PSLOTS = 3
QSLOTS = 3
STEPS = [(g, qb) for g in range(NG) for qb in range(NB)]
LEAD = 4
AHEAD = 8
AHEAD_FIRST = 12


def attention_order():
    tiles, ends = [], []
    for s, (g, qb) in enumerate(STEPS):
        if s == 0:
            tiles += [("qk", 0)] + [("v", t) for t in range(NT // 2)]
            tiles += [("qk", 1)] + [("v", t) for t in range(NT // 2, NT)]
        elif s + 1 < len(STEPS):
            tiles.append(("qk", s + 1))
        for i in range(TPB):
            for p in range(PAIRS):
                for c in range(qb + 1):
                    for u in range(2):
                        tiles.append(("max", s, 2 * p + u, i, c))
        tiles.append(("m", s))
        ends.append(len(tiles))
    order, at = [], 0

    def maxima(upto):
        nonlocal at
        while at < min(upto, len(tiles)):
            order.append(tiles[at])
            at += 1

    maxima(ends[0] + AHEAD_FIRST)
    late = []
    n = done = 0
    for s, (g, qb) in enumerate(STEPS):
        kts = TPB * (qb + 1)
        done += qb + 1
        last = len(STEPS) - 1
        goal = (done + LEAD) * len(tiles) // sum(qb + 1 for _, qb in STEPS)
        goal = min(max(goal, ends[min(s + 1, last)] + AHEAD), ends[min(s + QSLOTS - 1, last)])
        start = at
        for kt in range(kts):
            share = start + (goal - start) * (kt + 1) // kts
            order.append(("score", s, kt, 0))
            maxima(at + (share - at) // 3)
            order.append(("score", s, kt, 1))
            maxima(at + (share - at) // 2)
            if kt:
                order.append(("pv", s, kt - 1))
            maxima(share)
            n += 1
            while late and late[0][0] <= n:
                order.append(late.pop(0)[1])
        order.append(("pv", s, kts - 1))
        late += [(n + 3, ("yt", s)), (n + 6, ("yc", s))] + [(n + 9 + t, ("out", s, t)) for t in range(TPB)]
    order += [item for _, item in late]
    return order


ORDER = attention_order()
RING_KINDS = ("v", "qk", "max", "m", "yt", "yc", "out")
RING_NO = {item: n for n, item in enumerate(x for x in ORDER if x[0] in RING_KINDS)}
HI_NO = {item: n for n, item in enumerate(x for x in ORDER if x[0] in ("qk", "m", "yc"))}
SCORE_NO = {item[1:]: n for n, item in enumerate(x for x in ORDER if x[0] == "score")}
PV_NO = {item[1:]: n for n, item in enumerate(x for x in ORDER if x[0] == "pv")}
DIAG_NO = {k: n for n, k in enumerate(k for k in SCORE_NO if k[1] >= TPB * STEPS[k[0]][1])}
LAST_SCORE = [SCORE_NO[s, TPB * (qb + 1) - 1, 1] for s, (_, qb) in enumerate(STEPS)]
LAST_PV = [PV_NO[s, TPB * (qb + 1) - 1] for s, (_, qb) in enumerate(STEPS)]
RINGS, HIS, SCORES, PVS, DIAGS, NS = map(len, (RING_NO, HI_NO, SCORE_NO, PV_NO, DIAG_NO, STEPS))
TPS = KC * NB
QK_DMAS, M_DMAS = 18, 4


def macaron(nc, x, w_attn, b_attn, w_proj, b_proj, w1, w2, b2, b1_cols, bqk_cols, out):
    ctx = ExitStack()
    with ctx:
        def sb(name, shape, dt=F32):
            return ctx.enter_context(nc.sbuf_tensor(name, shape, dt))

        def sem(name):
            return ctx.enter_context(nc.semaphore(name))

        w1h, w1l = sb("w1h", [P, KC, F], F32R), sb("w1l", [P, KC, F], F32R)
        w2h, w2l = sb("w2h", [P, FT, C], F32R), sb("w2l", [P, FT, C], F32R)
        wqkh, wqkl = sb("wqkh", [P, KC, NG, P], F32R), sb("wqkl", [P, KC, NG, P], F32R)
        wvh, wvl = sb("wvh", [P, KC, C], F32R), sb("wvl", [P, KC, C], F32R)
        wph, wpl = sb("wph", [HG * D, NG, C], F32R), sb("wpl", [HG * D, NG, C], F32R)
        b1c = sb("b1c", [P, FT])
        bqk = sb("bqk", [P, NG])
        bvb, bpb, b2b = sb("bvb", [P, C]), sb("bpb", [P, C]), sb("b2b", [P, C])
        ident = sb("ident", [P, P])
        behind = sb("behind", [P, BLK])
        minus_half = sb("minus_half", [P, NT])
        xs = sb("xs", [P, NT, C])
        stats = sb("stats", [P, NT, 6])
        mv = sb("mv", [P, NT, 2])
        ve, rstd = sb("ve", [P, NT]), sb("rstd", [P, NT])
        xth, xtl = sb("xth", [P, KC, T], F32R), sb("xtl", [P, KC, T], F32R)
        wide = sb("wide", [P, 3072])
        pw = wide[:, :].rearrange("p (s u n) -> p s u n", s=PSLOTS, u=2)
        gel = wide[:, 0:2048].rearrange("p (s n) -> p s n", s=UPS)
        xn = wide[:, 2048:3072].rearrange("p (s n) -> p s n", s=XNS)
        qring = sb("qring", [P, QSLOTS, PAIRS, 2, BLK], F32R)
        kbuf = sb("kbuf", [P, 2, PAIRS, T], F32R)
        gsp = kbuf[:, 1].rearrange("p a (s n) -> p (a s) n", n=BLK)
        gh, gl = gsp[:, 0:UPS], gsp[:, UPS:2 * UPS]
        dnh, dnl = sb("dnh", [P, BLK], F32R), sb("dnl", [P, BLK], F32R)
        vall = sb("vall", [P, NT, H, VW])
        part = sb("part", [P, HG * TPB, NB])
        negm = sb("negm", [P, HG * TPB])
        mhl = sb("mhl", [64, BLK], F32R)
        mh, ml = mhl[0:HG, :], mhl[32:32 + HG, :]
        ysb = sb("ysb", [P, BLK])
        rsum = sb("rsum", [P, TPB, HG])
        yn = sb("yn", [P, TPB, HG, D])
        yth, ytl = sb("yth", [HG * D, BLK], F32R), sb("ytl", [HG * D, BLK], F32R)

        def f32(ap):
            return ap.bitcast(F32)

        ring = [ctx.enter_context(nc.psum_tensor(f"ring{i}", [P, BLK], F32)) for i in range(RING)]
        quad = ctx.enter_context(nc.psum_tensor("quad", [P, 4, BLK], F32))
        pvb = ctx.enter_context(nc.psum_tensor("pvb", [P, BLK], F32))
        ups = ring + [pvb]

        s_w = sem("weights_in")
        s_const = sem("constants_set")
        s_split = sem("weights_split")
        s_bias = sem("bias_halved")
        s_x = [sem(f"x_in{i}") for i in range(NB)]
        s_out = sem("block_stored")
        s_stat = sem("stats_done")
        s_aggr = sem("moments_done")
        s_ve = sem("variance_eps")
        s_rstd = sem("rstd_done")
        s_xn = sem("xn_done")
        s_tp = sem("transposed")
        s_xth = sem("xt_high")
        s_xtl = sem("xt_low")
        s_pre = sem("bias_added")
        s_ones = sem("keys_ones_set")
        s_up = sem("hidden_done")
        s_gelu = sem("gelu_done")
        s_gh = sem("gelu_high")
        s_gl = sem("gelu_low")
        s_down = sem("down_done")
        s_res = sem("residual_done")
        s_full = sem("ring_full")
        s_free = sem("ring_free")
        s_hi = sem("high_done")
        s_qk = sem("qk_in")
        s_negm = sem("negm_done")
        s_m = sem("m_in")
        s_sc = sem("scores_done")
        s_exp = sem("exp_done")
        s_mask = sem("masked")
        s_pv = sem("pv_done")
        s_y = sem("y_copied")
        s_rs = sem("sums_inverted")

        WEIGHT_DMAS = 9
        CONSTS = 6

        def wait_apart(engine, sem, count):
            engine.wait_ge(sem, count)
            engine.sem_inc(s_apart[engine.engine], 1)

        s_apart = {e.engine: sem(f"waits_apart_{k}") for k, e in enumerate(
            (nc.sync, nc.gpsimd, nc.vector, nc.scalar, nc.tensor))}

        block = ctx.enter_context(nc.Block())

        @block.sync
        def _(sp):
            st1, st2 = xs[:, 0:8, :], xs[:, 8:16, :]
            sp.dma_start(st1.rearrange("p (k a) c -> p k (a c)", k=KC),
                         w1.rearrange("(k p) f -> p k f", p=P)).then_inc(s_w, 16)
            sp.dma_start(st2, w2.rearrange("(j p) c -> p j c", p=P)).then_inc(s_w, 16)
            sp.dma_start(wide[:, 0:1536].rearrange("p (k c) -> p k c", k=KC),
                         w_attn.rearrange("(k p) c -> p k c", p=P)).then_inc(s_w, 16)
            sp.dma_start(wide[0:HG * D, 1536:2560].rearrange("p (g c) -> p g c", g=NG),
                         w_proj.rearrange("(g p) c -> p g c", g=NG)).then_inc(s_w, 16)
            sp.dma_start(b1c[:, :], b1_cols).then_inc(s_w, 16)
            sp.dma_start(bqk[:, :], bqk_cols).then_inc(s_w, 16)
            sp.dma_start(bvb[:, :], b_attn[2 * C:3 * C].partition_broadcast(P)).then_inc(s_w, 16)
            sp.dma_start(bpb[:, :], b_proj.partition_broadcast(P)).then_inc(s_w, 16)
            sp.dma_start(b2b[:, :], b2.partition_broadcast(P)).then_inc(s_w, 16)
            sp.wait_ge(s_split, 1)
            for i in range(NB):
                sp.dma_start(xs[:, i * TPB:(i + 1) * TPB, :],
                             x[0, i * BLK:(i + 1) * BLK, :].rearrange("(t p) c -> p t c", p=P)).then_inc(s_x[i], 16)

            def send(b):
                for item in ORDER:
                    if item[0] == "qk":
                        n = item[1]
                        g, blk = STEPS[n]
                        wait_apart(sp, s_free, b * RINGS + RING_NO[item] + 1)
                        for p in range(PAIRS):
                            for j, src in enumerate((dnh, dnl, dnh)):
                                sp.dma_start(
                                    f32(kbuf[32 * j:32 * j + 32, g % 2, p, blk * BLK:(blk + 1) * BLK]),
                                    f32(src[64 + 32 * p:96 + 32 * p, :])).then_inc(s_qk, 16)
                        if n >= QSLOTS:
                            wait_apart(sp, s_sc, b * SCORES + LAST_SCORE[n - QSLOTS] + 1)
                        for h in range(HG):
                            p, u = h // 2, h % 2
                            for j, src in enumerate((dnh, dnh, dnl)):
                                r = 32 * j + D * u
                                sp.dma_start(f32(qring[r:r + D, n % QSLOTS, p, u, :]),
                                             f32(src[h * D:(h + 1) * D, :])).then_inc(s_qk, 16)
                with sp.Fori(0, NB) as i:
                    n = (b * 2 + 1) * NB + i
                    wait_apart(sp, s_res, n + 2)
                    sp.dma_start(out[b, bass.ds(i * BLK, BLK), :].rearrange("(t p) c -> p t c", p=P),
                                 xs[:, bass.ds(i * TPB, TPB), :]).then_inc(s_out, 16)

            with sp.Fori(0, B - 1) as b:
                send(b)
                wait_apart(sp, s_out, (b + 1) * (16 * NB))
                for i in range(NB):
                    sp.dma_start(xs[:, i * TPB:(i + 1) * TPB, :],
                                 x[b + 1, i * BLK:(i + 1) * BLK, :].rearrange("(t p) c -> p t c", p=P)
                                 ).then_inc(s_x[i], 16)
            send(B - 1)
            sp.wait_ge(s_out, 16 * B * NB)

        @block.gpsimd
        def _(gp):
            nc.gpsimd.memset(ident[:, :], 0.0).then_inc(s_const, 1)
            nc.gpsimd.memset(behind[:, :], 0.0).then_inc(s_const, 1)
            nc.gpsimd.memset(minus_half[:, :], -0.5).then_inc(s_const, 1)
            nc.gpsimd.memset(vall[:, :, :, D:VW], 1.0).then_inc(s_const, 1)
            gp.wait_ge(s_const, CONSTS - 2)
            nc.gpsimd.affine_select(out=ident[:, :], in_=ident[:, :], compare_op=ALU.not_equal, fill=1.0,
                                    base=0, pattern=[[-1, P]], channel_multiplier=1).then_inc(s_const, 1)
            nc.gpsimd.affine_select(out=behind[:, BLK - P:BLK], in_=behind[:, BLK - P:BLK],
                                    compare_op=ALU.is_ge, fill=NEVER,
                                    base=0, pattern=[[-1, P]], channel_multiplier=1).then_inc(s_const, 1)
            gp.wait_ge(s_w, 16 * WEIGHT_DMAS)
            nc.gpsimd.tensor_scalar(b2b[:, :], b2b[:, :], 0.5, None, ALU.mult).then_inc(s_bias, 1)
            gp.wait_ge(s_bias, 1)

            def inverse_deviation(b, l):
                wait_apart(gp, s_aggr, (b * 3 + (l + 1)) * NT)
                nc.gpsimd.tensor_scalar(ve[:, :], mv[:, :, 1], EPS, None, ALU.add).then_inc(s_ve, 1)
                gp.wait_ge(s_ve, b * 3 + (l + 1))
                nc.gpsimd.tensor_tensor(rstd[:, :], ve[:, :], minus_half[:, :], ALU.pow).then_inc(s_rstd, 1)

            def add_bias(b, l, bias):
                gp.wait_ge(s_xn, (b * 3 + (l + 1)) * NT)
                for t in range(TPB):
                    nc.gpsimd.tensor_tensor(xs[:, t * 4:t * 4 + 4, :], xs[:, t * 4:t * 4 + 4, :],
                                            bias[:, :].unsqueeze(1).broadcast_to([P, 4, C]),
                                            ALU.add).then_inc(s_pre, 1)

            with gp.Fori(0, B) as b:
                inverse_deviation(b, 0)
                add_bias(b, 0, b2b)
                wait_apart(gp, s_res, (b * 2 + 1) * NB + 1)
                wait_apart(gp, s_pre, (b * 3 + 1) * TPB)
                nc.gpsimd.memset(f32(kbuf[KK:P, 1, :, :]), 1.0).then_inc(s_ones, 1)
                wait_apart(gp, s_ones, b + 1)
                inverse_deviation(b, 1)
                add_bias(b, 1, bpb)
                for item in ORDER:
                    if item[0] == "m":
                        wait_apart(gp, s_free, b * RINGS + RING_NO[item] + 1)
                        for h in range(HG):
                            gp.dma_start(f32(qring[KK:KM, item[1] % QSLOTS, h // 2, h % 2, :]),
                                         f32(mhl[h:h + 33:32, :])).then_inc(s_m, 16)
                    elif item[1:] in DIAG_NO and item[0] == "score":
                        key = item[1:]
                        wait_apart(gp, s_exp, b * SCORES + SCORE_NO[key] + 1)
                        tri = pw[:, SCORE_NO[key] % PSLOTS, :, 0:P]
                        nc.gpsimd.affine_select(out=tri, in_=tri, compare_op=ALU.is_ge, fill=0.0, base=0,
                                                pattern=[[0, 2], [1, P]], channel_multiplier=-1).then_inc(s_mask, 1)
                inverse_deviation(b, 2)
                add_bias(b, 2, b2b)

        @block.vector
        def _(dve):
            dve.wait_ge(s_w, 16 * WEIGHT_DMAS)
            parts = []
            for hi, lo, src in (
                (w1h[:, :, :], w1l[:, :, :], xs[:, 0:8, :].rearrange("p (k a) c -> p k (a c)", k=KC)),
                (w2h[:, :, :], w2l[:, :, :], xs[:, 8:16, :]),
                (wph[:, :, :], wpl[:, :, :], wide[0:HG * D, 1536:2560].rearrange("p (g c) -> p g c", g=NG)),
                (wvh[:, :, :], wvl[:, :, :], wide[:, 0:1536].rearrange("p (k c) -> p k c", k=KC)[:, :, 2 * C:]),
            ):
                parts.append((hi, lo, src))
            for q in range(2):
                for k in range(KC):
                    src = wide[:, k * 768 + q * C:k * 768 + (q + 1) * C].rearrange("p (g c) -> p g c", g=NG)
                    parts.append((wqkh[:, k, :, 64 * q:64 * q + 64], wqkl[:, k, :, 64 * q:64 * q + 64], src))
            for n, (hi, lo, src) in enumerate(parts):
                nc.vector.tensor_copy(hi, src).then_inc(s_gh, 1)
            dve.wait_ge(s_gh, len(parts))
            for n, (hi, lo, src) in enumerate(parts):
                ins = nc.vector.tensor_tensor(lo, src, f32(hi), ALU.subtract)
                if n < len(parts) - 1:
                    ins.then_inc(s_gl, 1)
                else:
                    ins.then_inc(s_split, 1)
            nc.vector.memset(pvb[:, :], 0.0).then_inc(s_split, 1)
            nc.vector.memset(f32(qring[:, :, :, :, :]), 0.0).then_inc(s_split, 1)
            nc.vector.memset(f32(kbuf[KK:P, 0, :, :]), 1.0).then_inc(s_split, 1)
            GH0, GL0 = len(parts), len(parts) - 1
            nc.vector.memset(part[:, :, :], 0.0).then_inc(s_res, 1)

            def layer_norm(b, l):
                for t in range(NT):
                    if l == 0 and t % TPB == 0:
                        dve.wait_ge(s_x[t // TPB], (b + 1) * 16)
                    if l == 1 and t == 0:
                        dve.wait_ge(s_res, (b * 2 + 1) * NB + 1)
                    if l == 2 and t == 0:
                        dve.wait_ge(s_free, (b + 1) * RINGS)
                    nc.vector.bn_stats(stats[:, t, :], xs[:, t, :]).then_inc(s_stat, 1)
                for t in range(NT):
                    wait_apart(dve, s_stat, (b * 3 + l) * NT + t + 1)
                    nc.vector.bn_aggr(mv[:, t, :], stats[:, t, :]).then_inc(s_aggr, 1)
                dve.wait_ge(s_rstd, b * 3 + l + 1)

                def normalise(blk):
                    for t in range(blk * TPB, (blk + 1) * TPB):
                        if t >= XNS:
                            dve.wait_ge(s_tp, (b * 3 + l) * TPS + KC * ((t - XNS) // TPB + 1))
                        nc.vector.tensor_scalar(xn[:, t % XNS, :], xs[:, t, :], mv[:, t, 0:1], rstd[:, t:t + 1],
                                                ALU.subtract, ALU.mult).then_inc(s_xn, 1)

                normalise(0)
                for blk in range(NB):
                    if blk + 1 < NB:
                        normalise(blk + 1)
                    for k in range(KC):
                        n = blk * KC + k
                        cols = slice(blk * BLK, (blk + 1) * BLK)
                        dve.wait_ge(s_xth, (b * 3 + l) * TPS + n + 1)
                        nc.vector.tensor_tensor(xtl[:, k, cols], ring[n % RING][:, :], f32(xth[:, k, cols]),
                                                ALU.subtract).then_inc(s_xtl, 1)

            def feed_forward(b, f):
                with dve.Fori(0, NB) as i:
                    n = nc.vector.snap((b * 2 + f) * NB + i)
                    for j in range(FT):
                        slot = j % UPS
                        dve.wait_ge(s_gelu, n * FT + UPS + j + 1)
                        dve.wait_ge(s_down, n * FT + j + 1)
                        nc.vector.tensor_copy(gh[:, slot, :], gel[:, slot, :]).then_inc(s_gh, 1)
                        dve.wait_ge(s_gh, n * FT + GH0 + j + 1)
                        nc.vector.tensor_tensor(gl[:, slot, :], gel[:, slot, :], f32(gh[:, slot, :]),
                                                ALU.subtract).then_inc(s_gl, 1)
                    dve.wait_ge(s_down, n * FT + UPS + FT)
                    dve.wait_ge(s_pre, b * 3 * TPB + (2 * f + 1) * TPB)
                    rows = xs[:, bass.ds(i * TPB, TPB), :]
                    nc.vector.scalar_tensor_tensor(rows, quad[:, :, 0:C], 0.5, rows,
                                                   ALU.mult, ALU.add).then_inc(s_res, 1)

            def attention(b):
                for item in ORDER:
                    kind = item[0]
                    if kind not in RING_KINDS:
                        continue
                    r = RING_NO[item]
                    bank = ring[r % RING]
                    done = b * RINGS + r
                    if kind != "max":
                        dve.wait_ge(s_full, done + 1)
                    if kind == "v":
                        t = item[1]
                        nc.vector.tensor_tensor(
                            vall[:, t, :, 0:D], bank[:, 0:C].rearrange("p (h d) -> p h d", h=H),
                            bvb[:, :].rearrange("p (h d) -> p h d", h=H), ALU.add).then_inc(s_free, 1)
                    elif kind == "qk":
                        g, _ = STEPS[item[1]]
                        dve.wait_ge(s_hi, b * HIS + HI_NO[item] + 1)
                        if item[1]:
                            dve.wait_ge(s_qk, (b * NS + item[1]) * QK_DMAS * 16)
                        nc.vector.scalar_tensor_tensor(dnl[:, :], bank[:, :], bqk[:, g:g + 1], f32(dnh[:, :]),
                                                       ALU.add, ALU.subtract).then_inc(s_free, 1)
                    elif kind == "max":
                        _, s, h, i, c = item
                        qb = STEPS[s][1]
                        row = part[:, i * HG + h, c:c + 1]
                        if (h, i, c) == (0, 0, 0) and s:
                            dve.wait_ge(s_negm, b * NS + s)
                        if c < qb:
                            dve.wait_ge(s_full, done + 1)
                            nc.vector.tensor_reduce(row, bank[:, :], axis=AX.X, op=ALU.max).then_inc(s_free, 1)
                        else:
                            w = P * (i + 1)
                            wait_apart(dve, s_full, done + 1)
                            nc.vector.tensor_tensor_reduce(
                                out=bank[:, 0:w], in0=bank[:, 0:w], in1=behind[:, BLK - w:BLK], scale=1.0,
                                scalar=NEVER, op0=ALU.add, op1=ALU.max, accum_out=row).then_inc(s_free, 1)
                        if (h, i, c) == (HG - 1, TPB - 1, qb):
                            dve.wait_ge(s_free, done + 1)
                            if s:
                                dve.wait_ge(s_full, b * RINGS + RING_NO["m", s - 1] + 1)
                            nc.vector.tensor_reduce(negm[:, :], part[:, :, 0:qb + 1], axis=AX.X, op=ALU.max,
                                                    negate=True).then_inc(s_negm, 1)
                    elif kind == "m":
                        dve.wait_ge(s_hi, b * HIS + HI_NO[item] + 1)
                        if item[1]:
                            dve.wait_ge(s_m, (b * NS + item[1]) * M_DMAS * 16)
                        nc.vector.tensor_tensor(ml, bank[0:HG, :], f32(mh),
                                                ALU.subtract).then_inc(s_free, 1)
                    elif kind == "yt":
                        s = item[1]
                        heads = bank[:, :].rearrange("p (t h e) -> p t h e", t=TPB, h=HG)
                        nc.vector.reciprocal(rsum[:, :, :], heads[:, :, :, D]).then_inc(s_rs, 1)
                        dve.wait_ge(s_rs, b * NS + s + 1)
                        nc.vector.tensor_tensor(yn[:, :, :, :], heads[:, :, :, 0:D],
                                                rsum[:, :, :].unsqueeze(3).broadcast_to([P, TPB, HG, D]),
                                                ALU.mult).then_inc(s_free, 1)
                    elif kind == "yc":
                        dve.wait_ge(s_hi, b * HIS + HI_NO[item] + 1)
                        nc.vector.tensor_tensor(ytl[:, :], bank[0:HG * D, :], f32(yth[:, :]),
                                                ALU.subtract).then_inc(s_free, 1)
                    elif kind == "out":
                        _, s, t = item
                        g, qb = STEPS[s]
                        if g:
                            dve.wait_ge(s_free, b * RINGS + RING_NO["out", s - NB, t] + 1)
                        else:
                            dve.wait_ge(s_pre, (b * 3 + 2) * TPB)
                        tile = xs[:, qb * TPB + t, :]
                        nc.vector.tensor_tensor(tile, bank[:, 0:C], tile, ALU.add).then_inc(s_free, 1)

            with dve.Fori(0, B) as b:
                layer_norm(b, 0)
                feed_forward(b, 0)
                layer_norm(b, 1)
                attention(b)
                layer_norm(b, 2)
                feed_forward(b, 1)

        @block.scalar
        def _(act):
            act.wait_ge(s_split, 4)
            act.wait_ge(s_const, CONSTS)
            nc.scalar.activation(ysb[:, 0:1], ident[:, 0:1], ACT.Copy).then_inc(s_gelu, UPS)

            def layer_norm(b, l):
                for n in range(TPS):
                    blk, k = n // KC, n % KC
                    act.wait_ge(s_tp, (b * 3 + l) * TPS + n + 1)
                    nc.scalar.activation(xth[:, k, blk * BLK:(blk + 1) * BLK], ring[n % RING][:, :],
                                         ACT.Copy).then_inc(s_xth, 1)

            def feed_forward(b, f):
                with act.Fori(0, NB) as i:
                    n = nc.scalar.snap((b * 2 + f) * NB + i)
                    for j in range(FT):
                        act.wait_ge(s_up, n * FT + j + 1)
                        act.wait_ge(s_gl, n * FT + GLF + j)
                        nc.scalar.activation(gel[:, j % UPS, :], ups[j % UPS][:, :], ACT.Gelu,
                                             bias=b1c[:, j:j + 1]).then_inc(s_gelu, 1)

            def attention(b):
                for item in ORDER:
                    kind = item[0]
                    if kind in ("qk", "m", "yc"):
                        bank = ring[RING_NO[item] % RING]
                        act.wait_ge(s_full, b * RINGS + RING_NO[item] + 1)
                        if kind == "qk":
                            if item[1]:
                                act.wait_ge(s_qk, (b * NS + item[1]) * QK_DMAS * 16)
                            g, _ = STEPS[item[1]]
                            nc.scalar.activation(dnh[:, :], bank[:, :], ACT.Identity,
                                                 bias=bqk[:, g:g + 1]).then_inc(s_hi, 1)
                        elif kind == "m":
                            if item[1]:
                                act.wait_ge(s_m, (b * NS + item[1]) * M_DMAS * 16)
                            nc.scalar.activation(mh, bank[0:HG, :], ACT.Copy).then_inc(s_hi, 1)
                        else:
                            nc.scalar.activation(yth[:, :], bank[0:HG * D, :], ACT.Copy).then_inc(s_hi, 1)
                    elif kind == "score":
                        _, s, kt, p = item
                        n = SCORE_NO[s, kt, p]
                        w = BLK - max(0, kt - TPB * STEPS[s][1]) * P
                        act.wait_ge(s_sc, b * SCORES + n + 1)
                        if n >= PSLOTS:
                            act.wait_ge(s_pv, b * PVS + (n - PSLOTS) // PAIRS + 1)
                        half = n % 2
                        nc.scalar.activation(pw[:, n % PSLOTS, :, 0:w], quad[:, 2 * half:2 * half + 2, 0:w],
                                             ACT.Exp, scale=SCALE).then_inc(s_exp, 1)
                    elif kind == "pv" and PV_NO[item[1:]] == LAST_PV[item[1]]:
                        s = item[1]
                        act.wait_ge(s_pv, b * PVS + LAST_PV[s] + 1)
                        if s:
                            act.wait_ge(s_full, b * RINGS + RING_NO["yt", s - 1] + 1)
                        nc.scalar.activation(ysb[:, :], pvb[:, :], ACT.Copy).then_inc(s_y, 1)

            GLF = 7 - UPS + 1
            with act.Fori(0, B) as b:
                layer_norm(b, 0)
                feed_forward(b, 0)
                layer_norm(b, 1)
                attention(b)
                layer_norm(b, 2)
                feed_forward(b, 1)

        @block.tensor
        def _(pe):
            def transpose(out_ap, in_ap):
                return nc.tensor.matmul(out_ap, in_ap, ident[:, :], start=True, stop=True, is_transpose=True)

            def product(out_ap, ah, al, bh, bl, start, stop):
                for n, (a, c) in enumerate(((ah, bh), (ah, bl), (al, bh))):
                    last = nc.tensor.matmul(out_ap, a, c, start=start and n == 0, stop=stop and n == 2)
                return last

            pe.wait_ge(s_split, 4)
            pe.wait_ge(s_const, CONSTS)
            transpose(ring[0][:, 0:P], ident[:, :]).then_inc(s_down, UPS)

            def layer_norm(b, l):
                for n in range(TPS):
                    blk, k = n // KC, n % KC
                    if k == 0:
                        pe.wait_ge(s_xn, (b * 3 + l) * NT + (blk + 1) * TPB)
                    if n >= RING:
                        pe.wait_ge(s_xtl, (b * 3 + l) * TPS + n - RING + 1)
                    for t in range(TPB):
                        last = transpose(ring[n % RING][:, t * P:(t + 1) * P],
                                                   xn[:, (blk * TPB + t) % XNS, k * P:(k + 1) * P])
                    last.then_inc(s_tp, 1)

            def feed_forward(b, f):
                wait_apart(pe, s_xtl, (b * 3 + 2 * f + 1) * TPS)
                with pe.Fori(0, NB) as i:
                    n = nc.tensor.snap((b * 2 + f) * NB + i)
                    cols = bass.ds(i * BLK, BLK)

                    def up(j):
                        pe.wait_ge(s_gelu, n * FT + j + 1)
                        rows = slice(j * P, (j + 1) * P)
                        for k in range(KC):
                            last = product(ups[j % UPS][:, :], w1h[:, k, rows], w1l[:, k, rows],
                                           xth[:, k, cols], xtl[:, k, cols], k == 0, k == KC - 1)
                        last.then_inc(s_up, 1)

                    def down(j):
                        pe.wait_ge(s_gl, n * FT + 7 + j + 1)
                        if j == 0:
                            pe.wait_ge(s_res, n + 1)
                        for t in range(TPB):
                            toks = slice(t * P, (t + 1) * P)
                            last = product(quad[:, t, 0:C], gh[:, j % UPS, toks], gl[:, j % UPS, toks],
                                           w2h[:, j, :], w2l[:, j, :], j == 0, j == FT - 1)
                        last.then_inc(s_down, 1)

                    up(0)
                    up(1)
                    for j in range(FT):
                        if j + 2 < FT:
                            up(j + 2)
                        down(j)

            def attention(b):
                for item in ORDER:
                    kind = item[0]
                    if kind in RING_KINDS:
                        r = RING_NO[item]
                        bank = ring[r % RING]
                        after = {"yc": ("yt", *item[1:2]), "out": ("yc", *item[1:2])}.get(kind)
                        need = max(r - RING, RING_NO[after] if after else -1)
                        if need >= 0:
                            if kind == "yc":
                                wait_apart(pe, s_free, b * RINGS + need + 1)
                            else:
                                pe.wait_ge(s_free, b * RINGS + need + 1)
                    if kind == "v":
                        t = item[1]
                        toks = slice(t * P, (t + 1) * P)
                        for k in range(KC):
                            last = product(bank[:, 0:C], xth[:, k, toks], xtl[:, k, toks],
                                           wvh[:, k, :], wvl[:, k, :], k == 0, k == KC - 1)
                        last.then_inc(s_full, 1)
                    elif kind == "qk":
                        g, blk = STEPS[item[1]]
                        if item[1] == 0:
                            pe.wait_ge(s_xtl, (b * 3 + 2) * TPS)
                        cols = slice(blk * BLK, (blk + 1) * BLK)
                        for k in range(KC):
                            last = product(bank[:, :], wqkh[:, k, g, :], wqkl[:, k, g, :],
                                           xth[:, k, cols], xtl[:, k, cols], k == 0, k == KC - 1)
                        last.then_inc(s_full, 1)
                    elif kind == "max":
                        _, s, h, i, c = item
                        g, qb = STEPS[s]
                        p, u = h // 2, h % 2
                        if (h, i, c) == (0, 0, 0):
                            pe.wait_ge(s_qk, (b * NS + s + 1) * QK_DMAS * 16)
                        w = BLK if c < qb else P * (i + 1)
                        nc.tensor.matmul(bank[:, 0:w], qring[0:KK, s % QSLOTS, p, u, i * P:(i + 1) * P],
                                         kbuf[0:KK, g % 2, p, c * BLK:c * BLK + w],
                                         start=True, stop=True).then_inc(s_full, 1)
                    elif kind == "m":
                        wait_apart(pe, s_negm, b * NS + item[1] + 1)
                        for i in range(TPB):
                            last = transpose(bank[0:HG, i * P:(i + 1) * P],
                                                       negm[:, i * HG:(i + 1) * HG])
                        last.then_inc(s_full, 1)
                    elif kind == "score":
                        _, s, kt, p = item
                        g, qb = STEPS[s]
                        n = SCORE_NO[s, kt, p]
                        off = max(0, kt - TPB * qb) * P
                        if kt == 0 and p == 0:
                            pe.wait_ge(s_m, (b * NS + s + 1) * M_DMAS * 16)
                        if (g, qb, kt, p) == (1, 0, 0, 0):
                            pe.wait_ge(s_ones, b + 1)
                        if n >= 2:
                            pe.wait_ge(s_exp, b * SCORES + n - 1)
                        for u in range(2):
                            last = nc.tensor.matmul(quad[:, 2 * (n % 2) + u, 0:BLK - off],
                                                    kbuf[0:KM, g % 2, p, kt * P:(kt + 1) * P],
                                                    qring[0:KM, s % QSLOTS, p, u, off:BLK], start=True, stop=True)
                        last.then_inc(s_sc, 1)
                    elif kind == "pv":
                        _, s, kt = item
                        g, qb = STEPS[s]
                        off = max(0, kt - TPB * qb) * P
                        pe.wait_ge(s_exp, b * SCORES + SCORE_NO[s, kt, 1] + 1)
                        if kt >= TPB * qb:
                            pe.wait_ge(s_mask, b * DIAGS + DIAG_NO[s, kt, 1] + 1)
                        if kt == 0 and s:
                            pe.wait_ge(s_y, b * NS + s)
                        for h in range(HG):
                            p, u = h // 2, h % 2
                            last = nc.tensor.matmul(pvb[32 * h:32 * h + VW, off:BLK], vall[:, kt, HG * g + h, :],
                                                    pw[:, SCORE_NO[s, kt, p] % PSLOTS, u, 0:BLK - off],
                                                    start=kt == 0, stop=kt == TPB * (qb + 1) - 1)
                        last.then_inc(s_pv, 1)
                    elif kind == "yt":
                        pe.wait_ge(s_y, b * NS + item[1] + 1)
                        for t in range(TPB):
                            last = transpose(bank[:, t * P:(t + 1) * P], ysb[:, t * P:(t + 1) * P])
                        last.then_inc(s_full, 1)
                    elif kind == "yc":
                        for t in range(TPB):
                            last = transpose(bank[0:HG * D, t * P:(t + 1) * P],
                                                       yn[:, t, :, :].rearrange("p h d -> p (h d)"))
                        last.then_inc(s_full, 1)
                    elif kind == "out":
                        _, s, t = item
                        g = STEPS[s][0]
                        toks = slice(t * P, (t + 1) * P)
                        product(bank[:, 0:C], yth[:, toks], ytl[:, toks], wph[:, g, :], wpl[:, g, :],
                                True, True).then_inc(s_full, 1)

            with pe.Fori(0, B) as b:
                layer_norm(b, 0)
                feed_forward(b, 0)
                layer_norm(b, 1)
                attention(b)
                layer_norm(b, 2)
                feed_forward(b, 1)


_INS = ["L0_attn_x", "L0_attn_W_attn", "L0_attn_b_attn", "L0_attn_W_proj", "L0_attn_b_proj",
        "L0_ffn_w1", "L0_ffn_w2", "L0_ffn_b2"]


def kernel(**inputs):
    import numpy as _np
    import concourse.bacc as _bacc
    from concourse import mybir as _mybir
    from concourse.bass_utils import run_bass_kernel_spmd as _run

    nc = _bacc.Bacc("TRN2", target_bir_lowering=False, num_devices=1)
    laid = {name: _np.ascontiguousarray(inputs[name]) for name in _INS}
    laid["b1_cols"] = _np.ascontiguousarray(_np.asarray(inputs["L0_ffn_b1"]).reshape(FT, P).T)
    qk = _np.asarray(inputs["L0_attn_b_attn"])[:2 * C].reshape(2, NG, HG * D)
    laid["bqk_cols"] = _np.ascontiguousarray(qk.transpose(0, 2, 1).reshape(P, NG))
    arrays, args = {}, []
    for name, a in laid.items():
        arrays[f"in_{name}"] = a
        args.append(nc.dram_tensor(f"in_{name}", a.shape, _mybir.dt.from_np(a.dtype), kind="ExternalInput").ap())
    args.append(nc.dram_tensor("out_0", (B, T, C), _mybir.dt.float32, kind="ExternalOutput").ap())
    macaron(nc, *args)
    r = _run(nc, [arrays], core_ids=[0])
    return r.results[0]["out_0"]
```
